# Optimizing a Trainium2 kernel written in Bass

```python
import numpy as np
import jax
import jax.numpy as jnp

def _softmax(x, axis=-1):
    return jax.nn.softmax(x, axis=axis)

def _gelu(x):
    return jax.nn.gelu(x, approximate=True)

def _silu(x):
    return jax.nn.silu(x)

def _sigmoid(x):
    return jax.nn.sigmoid(x)

def _layernorm(x, axis=-1, eps=1e-05):
    m = jnp.mean(x, axis=axis, keepdims=True)
    v = jnp.var(x, axis=axis, keepdims=True)
    return (x - m) / jnp.sqrt(v + eps)

def _scatter_add(tgt, idx, src, axis=0):
    return tgt.at[idx].add(src)

def _segment_sum(src, seg, n):
    return jax.ops.segment_sum(src, seg, n)
kernel_name = 'mk_gnn_ffn_d1_gnn_r32_3d698f'

def setup_inputs(seed: int=0):
    np.random.seed(seed)
    _w = jnp.asarray

    def _rec_inputs():
        import jax
        import jax.numpy as jnp
        _gk = jax.random.key(seed)
        x = -0.0005963 + 1.001 * jax.random.normal(jax.random.fold_in(_gk, 1), (96, 1024), jnp.float32)
        src = jax.random.randint(jax.random.fold_in(_gk, 2), (3072,), 0, 96, jnp.int32)
        dst = jnp.minimum((96 * jax.random.uniform(jax.random.fold_in(_gk, 3), (3072,)) ** 2.0).astype(jnp.int32), 3071)
        _o = jnp.argsort(dst, stable=True)
        src = src[_o]
        dst = dst[_o]
        edge_type_5 = jax.random.randint(jax.random.fold_in(_gk, 12), (3072,), 0, 5, jnp.int32)
        return (x, src, dst, edge_type_5)
    x, src, dst, edge_type_5 = _rec_inputs()

    def _L0_gnn_setup():
        import jax, jax.numpy as jnp
        import numpy as np
        N = 96
        E = 3072
        IN_F = 1024
        OUT_F = 1024
        H = 16
        D = OUT_F // H
        NUM_ETYPES = 4

        def _build_mask(edge_index, edge_type, edge_type_weights, dtype):
            src, dst = (edge_index[0], edge_index[1])
            w = jax.nn.softplus(edge_type_weights)
            mask = jnp.full((N, N), -jnp.inf, dtype=dtype)
            mask = mask.at[src, dst].set(w[edge_type - 1])
            diag = jnp.diagonal(mask)
            idx = jnp.arange(N)
            mask = mask.at[idx, idx].set(jnp.where(jnp.isneginf(diag), w[3], diag))
            return mask
        key = jax.random.key(seed)
        ks = jax.random.split(key, 20)
        p = lambda k, shape: jax.random.normal(k, shape, dtype=jnp.float32) * 0.02
        return {'x': jax.random.normal(ks[0], (N, IN_F), dtype=jnp.float32), 'edge_index': jax.random.randint(ks[1], (2, E), 0, N), 'edge_type': jax.random.randint(ks[2], (E,), 1, NUM_ETYPES + 1), 'edge_type_weights': jnp.ones((NUM_ETYPES,), jnp.float32) + 0.1 * jax.random.normal(ks[3], (NUM_ETYPES,), dtype=jnp.float32), 'wq': p(ks[4], (OUT_F, IN_F)), 'bq': p(ks[5], (OUT_F,)), 'wk': p(ks[6], (OUT_F, IN_F)), 'bk': p(ks[7], (OUT_F,)), 'wv': p(ks[8], (OUT_F, IN_F)), 'bv': p(ks[9], (OUT_F,)), 'wiq': p(ks[10], (OUT_F, OUT_F)), 'biq': p(ks[11], (OUT_F,)), 'wik': p(ks[12], (OUT_F, OUT_F)), 'bik': p(ks[13], (OUT_F,)), 'wiv': p(ks[14], (OUT_F, OUT_F)), 'biv': p(ks[15], (OUT_F,)), 'wo': p(ks[16], (OUT_F, OUT_F)), 'bo': p(ks[17], (OUT_F,))}
    _L0_gnn_all = _L0_gnn_setup()
    _L0_gnn_in = {k: v for k, v in _L0_gnn_all.items() if k in ('edge_type_weights', 'wq', 'bq', 'wk', 'bk', 'wv', 'bv', 'wiq', 'biq', 'wik', 'bik', 'wiv', 'biv', 'wo', 'bo')}
    del _L0_gnn_all

    def _L0_ffn_setup():
        import jax, jax.numpy as jnp
        import numpy as np
        NUM_EXPERTS = 64
        TOP_K = 8
        HIDDEN = 1024
        INTER = 768
        B, S = (2, 64)
        key = jax.random.key(seed)
        k1, k2, k3, k4 = jax.random.split(key, 4)
        hidden_states = jax.random.normal(k1, (B, S, HIDDEN), jnp.float32)
        gate = jax.random.normal(k2, (NUM_EXPERTS, HIDDEN), jnp.float32) * 0.02
        gate_up_proj = jax.random.normal(k3, (NUM_EXPERTS, 2 * INTER, HIDDEN), jnp.float32) * 0.02
        down_proj = jax.random.normal(k4, (NUM_EXPERTS, HIDDEN, INTER), jnp.float32) * 0.02
        return {'hidden_states': hidden_states, 'gate': gate, 'gate_up_proj': gate_up_proj, 'down_proj': down_proj}
    _L0_ffn_all = _L0_ffn_setup()
    _L0_ffn_in = {k: v for k, v in _L0_ffn_all.items() if k in ('gate', 'gate_up_proj', 'down_proj')}
    del _L0_ffn_all
    return {'x': x, 'src': src, 'dst': dst, 'edge_type_5': edge_type_5, 'L0_gnn_edge_type_weights': _L0_gnn_in['edge_type_weights'], 'L0_gnn_wq': _L0_gnn_in['wq'], 'L0_gnn_bq': _L0_gnn_in['bq'], 'L0_gnn_wk': _L0_gnn_in['wk'], 'L0_gnn_bk': _L0_gnn_in['bk'], 'L0_gnn_wv': _L0_gnn_in['wv'], 'L0_gnn_bv': _L0_gnn_in['bv'], 'L0_gnn_wiq': _L0_gnn_in['wiq'], 'L0_gnn_biq': _L0_gnn_in['biq'], 'L0_gnn_wik': _L0_gnn_in['wik'], 'L0_gnn_bik': _L0_gnn_in['bik'], 'L0_gnn_wiv': _L0_gnn_in['wiv'], 'L0_gnn_biv': _L0_gnn_in['biv'], 'L0_gnn_wo': _L0_gnn_in['wo'], 'L0_gnn_bo': _L0_gnn_in['bo'], 'L0_ffn_gate': _L0_ffn_in['gate'], 'L0_ffn_gate_up_proj': _L0_ffn_in['gate_up_proj'], 'L0_ffn_down_proj': _L0_ffn_in['down_proj']}

def reference(x, src, dst, edge_type_5, L0_gnn_edge_type_weights, L0_gnn_wq, L0_gnn_bq, L0_gnn_wk, L0_gnn_bk, L0_gnn_wv, L0_gnn_bv, L0_gnn_wiq, L0_gnn_biq, L0_gnn_wik, L0_gnn_bik, L0_gnn_wiv, L0_gnn_biv, L0_gnn_wo, L0_gnn_bo, L0_ffn_gate, L0_ffn_gate_up_proj, L0_ffn_down_proj):
    import jax
    import jax.numpy as jnp

    def _L0_gnn_ref(x, edge_index, edge_type, edge_type_weights, wq, bq, wk, bk, wv, bv, wiq, biq, wik, bik, wiv, biv, wo, bo):
        import jax, jax.numpy as jnp
        import numpy as np
        N = 96
        E = 3072
        IN_F = 1024
        OUT_F = 1024
        H = 16
        D = OUT_F // H
        NUM_ETYPES = 4

        def _build_mask(edge_index, edge_type, edge_type_weights, dtype):
            src, dst = (edge_index[0], edge_index[1])
            w = jax.nn.softplus(edge_type_weights)
            mask = jnp.full((N, N), -jnp.inf, dtype=dtype)
            mask = mask.at[src, dst].set(w[edge_type - 1])
            diag = jnp.diagonal(mask)
            idx = jnp.arange(N)
            mask = mask.at[idx, idx].set(jnp.where(jnp.isneginf(diag), w[3], diag))
            return mask
        q = x @ wq.T + bq
        k = x @ wk.T + bk
        v = x @ wv.T + bv
        q2 = (q @ wiq.T + biq).reshape(N, H, D).transpose(1, 0, 2)
        k2 = (k @ wik.T + bik).reshape(N, H, D).transpose(1, 0, 2)
        v2 = (v @ wiv.T + biv).reshape(N, H, D).transpose(1, 0, 2)
        mask = _build_mask(edge_index, edge_type, edge_type_weights, x.dtype)
        scale = 1.0 / np.sqrt(D).astype(np.float32)
        scores = jnp.einsum('hnd,hmd->hnm', q2, k2) * scale + mask[None]
        attn = jax.nn.softmax(scores, axis=-1)
        out = jnp.einsum('hnm,hmd->hnd', attn, v2)
        out = out.transpose(1, 0, 2).reshape(N, OUT_F)
        return out @ wo.T + bo

    def _L0_ffn_ref(hidden_states, gate, gate_up_proj, down_proj):
        import jax, jax.numpy as jnp
        import numpy as np
        NUM_EXPERTS = 64
        TOP_K = 8
        HIDDEN = 1024
        INTER = 768
        B, S = (2, 64)
        b, s, h = hidden_states.shape
        x = hidden_states.reshape(-1, h)
        router_logits = x @ gate.T
        probs = jax.nn.softmax(router_logits.astype(jnp.float32), axis=-1)
        topk_w, selected = jax.lax.top_k(probs, TOP_K)
        topk_w = topk_w / topk_w.sum(axis=-1, keepdims=True)
        topk_w = topk_w.astype(x.dtype)
        flat_experts = selected.reshape(-1)
        gather_indices = jnp.argsort(flat_experts, stable=True)
        token_counts = jnp.bincount(flat_experts, length=NUM_EXPERTS).astype(jnp.int32)
        x_perm = x[gather_indices // TOP_K]
        first_gemm = jax.lax.ragged_dot(x_perm, jnp.swapaxes(gate_up_proj, 1, 2), token_counts)
        intermediate = jax.nn.silu(first_gemm[:, :INTER]) * first_gemm[:, INTER:]
        second_gemm = jax.lax.ragged_dot(intermediate, jnp.swapaxes(down_proj, 1, 2), token_counts)
        unperm = jnp.zeros_like(second_gemm).at[gather_indices].set(second_gemm)
        out = (unperm.reshape(-1, TOP_K, h) * topk_w[..., None]).sum(axis=1)
        return out.reshape(b, s, h)
    edge_index = jnp.stack([src, dst])
    x = x + _L0_gnn_ref(_layernorm(x, axis=-1), edge_index, edge_type_5, L0_gnn_edge_type_weights, L0_gnn_wq, L0_gnn_bq, L0_gnn_wk, L0_gnn_bk, L0_gnn_wv, L0_gnn_bv, L0_gnn_wiq, L0_gnn_biq, L0_gnn_wik, L0_gnn_bik, L0_gnn_wiv, L0_gnn_biv, L0_gnn_wo, L0_gnn_bo)
    x = x + _L0_ffn_ref(_layernorm(x, axis=-1)[None], L0_ffn_gate, L0_ffn_gate_up_proj, L0_ffn_down_proj)[0]
    return x

_drawn_inputs = setup_inputs


def setup_inputs(seed=0):
    import zlib

    import numpy as np

    out = dict(_drawn_inputs(seed))
    spreads = {}
    factors = {'L0_gnn_edge_type_weights': 37.645,
     'L0_gnn_wq': 6.131,
     'L0_gnn_bq': 8.0,
     'L0_gnn_wk': 5.937,
     'L0_gnn_bk': 64.0,
     'L0_gnn_bv': 6.802,
     'L0_gnn_wiq': 6.047,
     'L0_gnn_biq': 8.0,
     'L0_gnn_wik': 6.108,
     'L0_gnn_bik': 64.0,
     'L0_gnn_biv': 4.385,
     'L0_gnn_bo': 2.828}
    for name, (base, spread) in spreads.items():
        noise = np.random.default_rng([zlib.crc32(name.encode()), seed]).standard_normal(out[name].shape)
        drawn = base * np.exp(spread * noise) if base else spread * noise
        out[name] = jnp.asarray(drawn.astype(out[name].dtype))
    for name, factor in factors.items():
        out[name] = (out[name] * factor).astype(out[name].dtype)
    return out
```

```python
import numpy as np

import concourse.bass as bass
from concourse import mybir
from contextlib import ExitStack

F32 = mybir.dt.float32
BF16 = mybir.dt.bfloat16
I32 = mybir.dt.int32
ALU = mybir.AluOpType
ACT = mybir.ActivationFunctionType
AX = mybir.AxisListType

P = 128
N = 96
D = 1024
KT = D // P
H, DH = 16, 64
EDGES = 3072
EB = EDGES // P
NE, INTER = 64, 768
TILES = INTER // P
UNIT = KT * P
CHUNK = 3 * UNIT
SLOTS = 12
GNN_UNITS = 7 * KT
GNN_CHUNKS = -(-GNN_UNITS // 3)
T = NE * TILES
U = 2 * TILES
TURNS = T // U
G4 = 4
EPS = 1e-5
ABSENT = -3.0e38
assert U == SLOTS and T % U == 0


def gnn_moe_kernel(nc, x, edges, edge_type_weights, bias_cols, biv, bo, gnn_stream, gate_w, expert_stream, out):
    ctx = ExitStack()
    with ctx:
        def sb(name, shape, dt=F32):
            return ctx.enter_context(nc.sbuf_tensor(name, shape, dt))

        def sem(name):
            return ctx.enter_context(nc.semaphore(name))

        ring = sb("ring", [P, SLOTS, CHUNK])
        x_rows = sb("x_rows", [N, D])
        x1_rows = sb("x1_rows", [N, D])
        norm_rows = sb("norm_rows", [N, D])
        norm_T = sb("norm_T", [P, KT, N])
        q_T = sb("q_T", [P, KT, N])
        k_T = sb("k_T", [P, KT, N])
        q2_T = sb("q2_T", [P, KT, N])
        k2_T = sb("k2_T", [P, KT, N])
        v2_rows = sb("v2_rows", [N, D])
        v_T = k_T
        heads_T = q_T
        y_T = k_T
        out_rows = v2_rows
        attn = sb("attn", [N, 4, G4, N])
        arena = sb("arena", [P, EB * N])
        pair_hit = arena[:, 0:EB * P // 2].bitcast(BF16).rearrange("p (b f) -> p b f", b=EB)
        src_hot = arena[:, 0:EB * N // 2].bitcast(BF16).rearrange("p (b n) -> p b n", b=EB)
        dst_hot = arena[:, EB * N // 2:EB * N].bitcast(BF16).rearrange("p (b n) -> p b n", b=EB)
        attn_T = arena[0:N, 0:4 * G4 * N].rearrange("p (g h n) -> p g h n", g=4, h=G4)
        router_w = sb("router_w", [P, KT, NE])
        bias_sb = sb("bias_sb", [P, 5, KT])
        ident = sb("ident", [P, P])
        ones = sb("ones", [N, P])
        later = sb("later", [P, P])
        zeros = sb("zeros", [P, G4 * N], BF16)
        node_id = sb("node_id", [P, N])
        block8 = sb("block8", [P, EB])
        edges_i = sb("edges_i", [P, 3, EB], I32)
        edges_f = sb("edges_f", [P, 3, EB])
        pair_key = sb("pair_key", [P, EB])
        edge_code = sb("edge_code", [P, EB])
        shadowed = sb("shadowed", [P, EB])
        code_part = sb("code_part", [N, 6, N])
        code_f = sb("code_f", [N, N])
        code_i = sb("code_i", [N, N], I32)
        mask = sb("mask", [N, N])
        etw = sb("etw", [N, 4])
        etw_abs = sb("etw_abs", [N, 4])
        etw_relu = sb("etw_relu", [N, 4])
        stats = sb("stats", [N, 2, 6])
        mean_var = sb("mean_var", [N, 2])
        ln_tmp = sb("ln_tmp", [N, 4])
        head_max = sb("head_max", [N, 4, G4])
        head_sum = sb("head_sum", [N, 4, G4])
        route = sb("route", [N, 3, NE])
        route_s = sb("route_s", [N, 6])
        top8 = sb("top8", [N, 8])
        route_w = sb("route_w", [N, NE + 2])
        gate_diag = sb("gate_diag", [N, 2, N])
        gate_row = sb("gate_row", [P, 2, N])
        silu_T = sb("silu_T", [P, 2, N])
        up_T = sb("up_T", [P, 2, N])
        inner_T = sb("inner_T", [P, 3, N])

        bank = [ctx.enter_context(nc.psum_tensor(f"bank{i}", [P, 512], F32)) for i in range(8)]

        def wide(b, rows=P):
            return bank[b][0:rows, 0:G4 * N].rearrange("p (g n) -> p g n", g=G4)

        SCORE_BANK = [4, 6, 5, 7]

        landed = [sem(f"landed{s}") for s in range(SLOTS)]
        x_landed = sem("x_landed")
        edges_landed = sem("edges_landed")
        etw_landed = sem("etw_landed")
        bias_landed = sem("bias_landed")
        bo_landed = sem("bo_landed")
        biv_landed = sem("biv_landed")
        router_landed = sem("router_landed")
        const_ready = sem("const_ready")
        pool_step = sem("pool_step")
        vector_step = sem("vector_step")
        scalar_step = sem("scalar_step")
        key_ready = sem("key_ready")
        pairs_ready = sem("pairs_ready")
        pairs_read = sem("pairs_read")
        onehot_ready = sem("onehot_ready")
        codes_ready = sem("codes_ready")
        codes_read = sem("codes_read")
        etw_abs_ready = sem("etw_abs_ready")
        softplus_ready = sem("softplus_ready")
        var_ready = sem("var_ready")
        std_ready = sem("std_ready")
        norm_ready = sem("norm_ready")
        norm_turned = sem("norm_turned")
        norm_T_ready = sem("norm_T_ready")
        unit_done = sem("unit_done")
        unit_copied = sem("unit_copied")
        scores_ready = sem("scores_ready")
        shifted = sem("shifted")
        exps_ready = sem("exps_ready")
        attn_ready = sem("attn_ready")
        attn_turned = sem("attn_turned")
        attn_T_ready = sem("attn_T_ready")
        v2_ready = sem("v2_ready")
        heads_done = sem("heads_done")
        heads_ready = sem("heads_ready")
        logits_ready = sem("logits_ready")
        logits_shift = sem("logits_shift")
        logits_exp = sem("logits_exp")
        diag_ready = sem("diag_ready")
        gate_spread = sem("gate_spread")
        gate_ready = sem("gate_ready")
        tile_ready = sem("tile_ready")
        silu_ready = sem("silu_ready")
        up_ready = sem("up_ready")
        inner_ready = sem("inner_ready")
        down_done = sem("down_done")
        y_ready = sem("y_ready")
        y_turned = sem("y_turned")
        out_ready = sem("out_ready")
        stored = sem("stored")

        block = ctx.enter_context(nc.Block())

        def slot_of(t):
            return (GNN_CHUNKS + t) % SLOTS

        def round_of(t):
            return (GNN_CHUNKS + t) // SLOTS + 1

        @block.sync
        def _(eng):
            eng.dma_start(x_rows[:, :], x).then_inc(x_landed, 16)

            def load_gnn(c):
                if c >= SLOTS:
                    eng.wait_ge(unit_done, 3 * (c - SLOTS + 1))
                n = min(3, GNN_UNITS - 3 * c)
                eng.dma_start(ring[:, c % SLOTS, 0:n * UNIT].rearrange("p (u f) -> p u f", u=n),
                              gnn_stream[3 * c:3 * c + n].rearrange("u p f -> p u f")).then_inc(landed[c % SLOTS], 16)

            for c in range(GNN_CHUNKS):
                load_gnn(c)

            for t in range(U):
                eng.wait_ge(unit_done, min(3 * (GNN_CHUNKS + t - SLOTS + 1), GNN_UNITS))
                eng.dma_start(ring[:, slot_of(t), :], expert_stream[t]).then_inc(landed[slot_of(t)], 16)
            with eng.Fori(1, TURNS) as i:
                for u in range(U):
                    eng.wait_ge(down_done, i * U + (u - U + 1))
                    eng.dma_start(ring[:, slot_of(u), :],
                                  expert_stream[bass.ds(i * U + u, 1)].rearrange("u p f -> p (u f)"))\
                       .then_inc(landed[slot_of(u)], 16)
            for half in range(2):
                eng.wait_ge(out_ready, half + 1)
                cols = slice(half * 512, half * 512 + 512)
                eng.dma_start(out[:, cols], out_rows[:, cols]).then_inc(stored, 16)
            eng.wait_ge(stored, 32)

        @block.gpsimd
        def _(eng):
            eng.memset(ident[:, :], 0.0).then_inc(pool_step, 1)
            eng.memset(later[:, :], 1.0).then_inc(pool_step, 1)
            eng.memset(ones[:, :], 1.0).then_inc(const_ready, 1)
            eng.memset(zeros[:, :], 0.0).then_inc(const_ready, 1)
            eng.memset(route_w[:, :], 0.0).then_inc(const_ready, 1)
            eng.iota(node_id[:, :], pattern=[[1, N]], base=0, channel_multiplier=0,
                     allow_small_or_imprecise_dtypes=True).then_inc(const_ready, 1)
            eng.iota(block8[:, :], pattern=[[8, EB]], base=8, channel_multiplier=0,
                     allow_small_or_imprecise_dtypes=True).then_inc(const_ready, 1)
            eng.wait_ge(pool_step, 2)
            eng.affine_select(out=ident[:, :], in_=ident[:, :], compare_op=ALU.not_equal, fill=1.0, base=0,
                              pattern=[[-1, P]], channel_multiplier=1).then_inc(const_ready, 1)
            eng.affine_select(out=later[:, :], in_=later[:, :], compare_op=ALU.is_gt, fill=0.0, base=0,
                              pattern=[[1, P]], channel_multiplier=-1).then_inc(const_ready, 1)

        CONSTS = 7

        @block.scalar
        def _(eng):
            eng.dma_start(edges_i[:, :, :], edges).then_inc(edges_landed, 16)
            eng.dma_start(etw[:, :], edge_type_weights.partition_broadcast(N)).then_inc(etw_landed, 16)
            eng.dma_start(bias_sb[:, :, :], bias_cols).then_inc(bias_landed, 16)
            eng.dma_start(x1_rows[:, :], bo.partition_broadcast(N)).then_inc(bo_landed, 16)
            eng.dma_start(v2_rows[:, :], biv.partition_broadcast(N)).then_inc(biv_landed, 16)
            eng.dma_start(router_w[:, :, :], gate_w).then_inc(router_landed, 16)

            def std(n):
                eng.wait_ge(var_ready, n)
                eng.activation(ln_tmp[:, 1:2], ln_tmp[:, 0:1], ACT.Sqrt).then_inc(std_ready, 1)

            def copy_norm_T(n):
                for half in range(2):
                    eng.wait_ge(norm_turned, 2 * n + half + 1)
                    eng.copy(norm_T[:, half * G4:half * G4 + G4, :], wide(2 + half)).then_inc(norm_T_ready, 1)

            std(1)
            eng.wait_ge(etw_abs_ready, 1)
            eng.activation(etw_abs[:, :], etw_abs[:, :], ACT.Exp, scale=-1.0).then_inc(scalar_step, 1)
            eng.wait_ge(scalar_step, 1)
            eng.activation(etw_abs[:, :], etw_abs[:, :], ACT.Ln, bias=1.0).then_inc(softplus_ready, 1)
            copy_norm_T(0)

            eng.wait_ge(bias_landed, 16)
            matrices = [(q_T, 0), (k_T, 1), (q2_T, 2), (k2_T, 3), (v_T, 4)]

            def copy_units(g):
                dest, b = matrices[g]
                for m in range(KT):
                    u = g * KT + m
                    eng.wait_ge(unit_done, u + 1)
                    eng.activation(dest[:, m, :], bank[u % 4][:, 0:N], ACT.Identity,
                                   bias=bias_sb[:, b, m:m + 1]).then_inc(unit_copied, 1)

            for g in range(4):
                copy_units(g)
            dest, b = matrices[4]
            for m in range(KT):
                if m % 2 == 1:
                    g = m // 2
                    eng.wait_ge(shifted, g + 1)
                    eng.activation(attn[:, g, :, :], attn[:, g, :, :], ACT.Exp).then_inc(exps_ready, 1)
                u = 4 * KT + m
                eng.wait_ge(unit_done, u + 1)
                eng.activation(dest[:, m, :], bank[u % 4][:, 0:N], ACT.Identity,
                               bias=bias_sb[:, b, m:m + 1]).then_inc(unit_copied, 1)
            for g in range(4):
                eng.wait_ge(attn_turned, g + 1)
                eng.copy(attn_T[:, g, :, :], wide(SCORE_BANK[g], N)).then_inc(attn_T_ready, 1)
            for half in range(2):
                eng.wait_ge(heads_done, half + 1)
                eng.copy(heads_T[:, half * G4:half * G4 + G4, :], wide(4 + half)).then_inc(heads_ready, 1)

            std(2)
            copy_norm_T(1)
            eng.wait_ge(logits_shift, 1)
            eng.activation(route[:, 1, :], route[:, 0, :], ACT.Exp, accum_out=route_s[:, 1:2]).then_inc(logits_exp, 1)
            eng.wait_ge(gate_spread, 1)
            eng.copy(gate_row[:, 0, :], bank[7][:, 0:N]).then_inc(gate_ready, 1)

            def turn(i, first):
                for u in range(U):
                    eng.wait_ge(tile_ready, i * U + (u + 1))
                    if not (first and u < 2):
                        eng.wait_ge(inner_ready, i * U + (u - 1))
                    eng.activation(silu_T[:, u % 2, :], bank[2 * (u % 2)][:, 0:N], ACT.Silu).then_inc(silu_ready, 1)
                    if u % TILES == 3:
                        e = u // TILES
                        eng.wait_ge(gate_spread, i * 2 + (e + 2))
                        if not (first and e == 0):
                            eng.wait_ge(inner_ready, i * U + TILES * e)
                        eng.copy(gate_row[:, (e + 1) % 2, :], bank[7][:, 0:N]).then_inc(gate_ready, 1)

            turn(0, True)
            with eng.Fori(1, TURNS) as i:
                turn(i, False)

            eng.wait_ge(down_done, T)
            for half in range(2):
                eng.copy(y_T[:, half * G4:half * G4 + G4, :], wide(4 + half)).then_inc(y_ready, 1)

        @block.vector
        def _(eng):
            steps = [0]

            def link(ins):
                steps[0] += 1
                ins.then_inc(vector_step, 1)
                eng.wait_ge(vector_step, steps[0])

            def layernorm(n, rows):
                for half in range(2):
                    link(eng.bn_stats(stats[:, half, :], rows[:, half * 512:half * 512 + 512]))
                link(eng.bn_aggr(mean_var[:, :], stats[:, :, :].rearrange("p a b -> p (a b)")))
                eng.tensor_scalar(ln_tmp[:, 0:1], mean_var[:, 1:2], EPS, None, ALU.add).then_inc(var_ready, 1)
                eng.wait_ge(std_ready, n)
                link(eng.reciprocal(ln_tmp[:, 2:3], ln_tmp[:, 1:2]))
                link(eng.tensor_scalar(ln_tmp[:, 3:4], ln_tmp[:, 2:3], ln_tmp[:, 2:3], ln_tmp[:, 0:1],
                                       ALU.mult, ALU.mult))
                link(eng.tensor_scalar(ln_tmp[:, 3:4], ln_tmp[:, 3:4], -0.5, 1.5, ALU.mult, ALU.add))
                link(eng.tensor_tensor(ln_tmp[:, 2:3], ln_tmp[:, 2:3], ln_tmp[:, 3:4], ALU.mult))
                for half in range(2):
                    cols = slice(half * 512, half * 512 + 512)
                    eng.tensor_scalar(norm_rows[:, cols], rows[:, cols], mean_var[:, 0:1], ln_tmp[:, 2:3],
                                      ALU.subtract, ALU.mult).then_inc(norm_ready, 1)

            eng.wait_ge(edges_landed, 16)
            link(eng.tensor_copy(edges_f[:, :, :], edges_i[:, :, :]))
            src, dst, kind = edges_f[:, 0, :], edges_f[:, 1, :], edges_f[:, 2, :]
            eng.scalar_tensor_tensor(pair_key[:, :], src, float(N), dst, ALU.mult, ALU.add).then_inc(key_ready, 1)
            eng.wait_ge(x_landed, 16)
            layernorm(1, x_rows)

            eng.wait_ge(etw_landed, 16)
            link(eng.tensor_scalar(etw_relu[:, :], etw[:, :], 0.0, None, ALU.max))
            eng.scalar_tensor_tensor(etw_abs[:, :], etw_relu[:, :], 2.0, etw[:, :], ALU.mult,
                                     ALU.subtract).then_inc(etw_abs_ready, 1)

            eng.wait_ge(const_ready, CONSTS)
            eng.wait_ge(key_ready, 1)
            for g in range(EB // 4):
                eng.wait_ge(pairs_ready, g + 1)
                for k in range(4):
                    b = 4 * g + k
                    last = eng.scalar_tensor_tensor(pair_hit[:, b, :], bank[4 + g % 4][:, k * P:k * P + P],
                                                    pair_key[:, b:b + 1], later[:, :], ALU.is_equal, ALU.mult,
                                                    accum_out=shadowed[:, b:b + 1])
                last.then_inc(pairs_read, 1)
            link(eng.tensor_scalar(edge_code[:, :], kind, 0.0, 4.0, ALU.is_equal, ALU.mult))
            link(eng.tensor_tensor(edge_code[:, :], edge_code[:, :], kind, ALU.add))
            link(eng.tensor_tensor(edge_code[:, :], edge_code[:, :], block8[:, :], ALU.add))
            eng.wait_ge(pairs_read, EB // 4)
            link(eng.scalar_tensor_tensor(edge_code[:, :], shadowed[:, :], 0.0, edge_code[:, :],
                                          ALU.is_equal, ALU.mult))
            node = node_id[:, :].unsqueeze(1).to_broadcast([P, EB, N])
            eng.tensor_tensor(src_hot, node, src.unsqueeze(2).to_broadcast([P, EB, N]),
                              ALU.is_equal).then_inc(onehot_ready, 1)
            link(eng.tensor_tensor(dst_hot, node, dst.unsqueeze(2).to_broadcast([P, EB, N]), ALU.is_equal))
            eng.tensor_tensor(dst_hot, dst_hot, edge_code[:, :].unsqueeze(2).to_broadcast([P, EB, N]),
                              ALU.mult).then_inc(onehot_ready, 1)
            eng.wait_ge(bo_landed, 16)
            link(eng.tensor_tensor(x1_rows[:, :], x1_rows[:, :], x_rows[:, :], ALU.add))
            for g in range(EB // 4):
                eng.wait_ge(codes_ready, g + 1)
                eng.tensor_reduce(code_part[:, g, :], wide(4 + g % 4, N).rearrange("p g n -> p n g"), AX.X,
                                  ALU.max).then_inc(codes_read, 1)
            eng.wait_ge(codes_read, EB // 4)
            link(eng.tensor_reduce(code_f[:, :], code_part[:, :, :].rearrange("p g n -> p n g"), AX.X, ALU.max))
            link(eng.scalar_tensor_tensor(code_f[:, :], ident[0:N, 0:N], 4.0, code_f[:, :], ALU.mult, ALU.max))
            link(eng.tensor_copy(code_i[:, :], code_f[:, :]))
            link(eng.tensor_scalar(code_i[:, :], code_i[:, :], 7, None, ALU.bitwise_and))
            link(eng.tensor_copy(code_f[:, :], code_i[:, :]))
            eng.wait_ge(softplus_ready, 1)
            link(eng.tensor_tensor(etw[:, :], etw_abs[:, :], etw_relu[:, :], ALU.add))
            link(eng.tensor_scalar(mask[:, :], code_f[:, :], 0.0, ABSENT, ALU.is_equal, ALU.mult))
            for c in range(1, 5):
                pick = attn[:, 0, c - 1, :]
                link(eng.tensor_scalar(pick, code_f[:, :], float(c), etw[:, c - 1:c], ALU.is_equal, ALU.mult))
                link(eng.tensor_tensor(mask[:, :], mask[:, :], pick, ALU.add))

            for g in range(4):
                eng.wait_ge(scores_ready, g + 1)
                link(eng.scalar_tensor_tensor(attn[:, g, :, :], wide(SCORE_BANK[g], N), float(DH) ** -0.5,
                                              mask[:, :].unsqueeze(1).to_broadcast([N, G4, N]),
                                              ALU.mult, ALU.add))
                link(eng.tensor_reduce(head_max[:, g, :], attn[:, g, :, :], AX.X, ALU.max))
                eng.tensor_tensor(attn[:, g, :, :], attn[:, g, :, :],
                                  head_max[:, g, :].unsqueeze(2).to_broadcast([N, G4, N]),
                                  ALU.subtract).then_inc(shifted, 1)
            for g in range(4):
                eng.wait_ge(exps_ready, g + 1)
                link(eng.tensor_reduce(head_sum[:, g, :], attn[:, g, :, :], AX.X, ALU.add))
                link(eng.reciprocal(head_sum[:, g, :], head_sum[:, g, :]))
                eng.tensor_tensor(attn[:, g, :, :], attn[:, g, :, :],
                                  head_sum[:, g, :].unsqueeze(2).to_broadcast([N, G4, N]),
                                  ALU.mult).then_inc(attn_ready, 1)

            eng.wait_ge(biv_landed, 16)
            for half in range(2):
                cols = slice(half * 512, half * 512 + 512)
                eng.wait_ge(unit_done, 5 * KT + 4 * (half + 1))
                eng.tensor_tensor(v2_rows[:, cols], bank[2 + half][0:N, :], v2_rows[:, cols],
                                  ALU.add).then_inc(v2_ready, 1)
            for half in range(2):
                cols = slice(half * 512, half * 512 + 512)
                eng.wait_ge(unit_done, 6 * KT + 4 * (half + 1))
                link(eng.tensor_tensor(x1_rows[:, cols], bank[half][0:N, :], x1_rows[:, cols], ALU.add))
            layernorm(2, x1_rows)

            eng.wait_ge(logits_ready, 1)
            link(eng.tensor_reduce(route_s[:, 0:1], bank[6][0:N, 0:NE], AX.X, ALU.max))
            eng.tensor_scalar(route[:, 0, :], bank[6][0:N, 0:NE], route_s[:, 0:1], None,
                              ALU.subtract).then_inc(logits_shift, 1)
            eng.wait_ge(logits_exp, 1)
            link(eng.reciprocal(route_s[:, 2:3], route_s[:, 1:2]))
            link(eng.tensor_scalar(route[:, 0, :], route[:, 1, :], route_s[:, 2:3], None, ALU.mult))
            link(eng.max(top8[:, :], route[:, 0, :]))
            link(eng.match_replace(route[:, 2, :], top8[:, :], route[:, 0, :], -1.0))
            link(eng.tensor_reduce(route_s[:, 3:4], top8[:, :], AX.X, ALU.add))
            link(eng.reciprocal(route_s[:, 4:5], route_s[:, 3:4]))
            link(eng.scalar_tensor_tensor(route[:, 1, :], route[:, 2, :], 0.0, route[:, 0, :], ALU.is_lt, ALU.mult))
            link(eng.tensor_scalar(route_w[:, 0:NE], route[:, 1, :], route_s[:, 4:5], None, ALU.mult))
            eng.tensor_scalar(gate_diag[:, 0, :], ident[0:N, 0:N], route_w[:, 0:1], None,
                              ALU.mult).then_inc(diag_ready, 1)

            def turn(i, first):
                for u in range(U):
                    e, j = u // TILES, u % TILES
                    eng.wait_ge(tile_ready, i * U + (u + 1))
                    if j == 0:
                        eng.wait_ge(gate_ready, i * 2 + (e + 1))
                    eng.tensor_tensor(up_T[:, u % 2, :], bank[2 * (u % 2) + 1][:, 0:N], gate_row[:, e, :],
                                      ALU.mult).then_inc(up_ready, 1)
                    eng.wait_ge(up_ready, i * U + (u + 1))
                    eng.wait_ge(silu_ready, i * U + (u + 1))
                    if not (first and u < 3):
                        eng.wait_ge(down_done, i * U + (u - 2))
                    eng.tensor_tensor(inner_T[:, u % 3, :], up_T[:, u % 2, :], silu_T[:, u % 2, :],
                                      ALU.mult).then_inc(inner_ready, 1)
                    if j == 1:
                        if not (first and e == 0):
                            eng.wait_ge(gate_spread, i * 2 + e)
                        col = 1 + e if first else bass.ds(i * 2 + (1 + e), 1)
                        w = route_w[:, col:col + 1] if first else route_w[:, col]
                        eng.tensor_scalar(gate_diag[:, (e + 1) % 2, :], ident[0:N, 0:N], w, None,
                                          ALU.mult).then_inc(diag_ready, 1)

            turn(0, True)
            with eng.Fori(1, TURNS) as i:
                turn(i, False)

            for half in range(2):
                cols = slice(half * 512, half * 512 + 512)
                eng.wait_ge(y_turned, half + 1)
                eng.tensor_tensor(out_rows[:, cols], bank[half][0:N, :], x1_rows[:, cols],
                                  ALU.add).then_inc(out_ready, 1)

        @block.tensor
        def _(eng):
            def turn_rows(n):
                for half in range(2):
                    eng.wait_ge(norm_ready, 2 * n + half + 1)
                    for m in range(G4):
                        k = half * G4 + m
                        last = eng.transpose(wide(2 + half)[:, m, :], norm_rows[:, k * P:k * P + P], ident[0:N, 0:N])
                    last.then_inc(norm_turned, 1)

            def spread_keys(g):
                if g >= 4:
                    eng.wait_ge(pairs_read, g - 3)
                for k in range(4):
                    b = 4 * g + k
                    last = eng.matmul(bank[4 + g % 4][:, k * P:k * P + P], pair_key[:, b:b + 1].to_broadcast([P, P]),
                                      ident[:, :], start=True, stop=True)
                last.then_inc(pairs_ready, 1)

            def place_codes(g):
                if g >= 4:
                    eng.wait_ge(codes_read, g - 3)
                for k in range(4):
                    b = 4 * g + k
                    last = eng.matmul(wide(4 + g % 4, N)[:, k, :], src_hot[:, b, :], dst_hot[:, b, :],
                                      start=True, stop=True)
                last.then_inc(codes_ready, 1)

            def unit_weights(u):
                c = u // 3
                eng.wait_ge(landed[c % SLOTS], 16 * (c // SLOTS + 1))
                return ring[:, c % SLOTS, (u % 3) * UNIT:(u % 3 + 1) * UNIT].rearrange("p (k o) -> p k o", k=KT)

            def project(g, src_T):
                for m in range(KT):
                    u = g * KT + m
                    if u >= 4:
                        eng.wait_ge(unit_copied, u - 3)
                    w = unit_weights(u)
                    for k in range(KT):
                        last = eng.matmul(bank[u % 4][:, 0:N], w[:, k, :], src_T[:, k, :],
                                          start=(k == 0), stop=(k == KT - 1))
                    last.then_inc(unit_done, 1)

            def project_rows(g, src_T, first_bank):
                for m in range(KT):
                    w = unit_weights(g * KT + m)
                    for k in range(KT):
                        last = eng.matmul(bank[first_bank + m // 4][0:N, (m % 4) * P:(m % 4 + 1) * P],
                                          src_T[:, k, :], w[:, k, :], start=(k == 0), stop=(k == KT - 1))
                    last.then_inc(unit_done, 1)

            def turn_attn(g):
                eng.wait_ge(attn_ready, g + 1)
                for h in range(G4):
                    last = eng.transpose(wide(SCORE_BANK[g], N)[:, h, :], attn[:, g, h, :], ident[0:N, 0:N])
                last.then_inc(attn_turned, 1)

            eng.wait_ge(const_ready, CONSTS)
            eng.wait_ge(key_ready, 1)
            for g in range(4):
                spread_keys(g)
            turn_rows(0)
            eng.wait_ge(norm_T_ready, 2)
            project(0, norm_T)
            for g in range(4, EB // 4):
                spread_keys(g)
            project(1, norm_T)
            eng.wait_ge(onehot_ready, 2)
            for g in range(4):
                place_codes(g)
            eng.wait_ge(unit_copied, KT)
            project(2, q_T)
            for g in range(4, EB // 4):
                place_codes(g)
            eng.wait_ge(unit_copied, 2 * KT)
            project(3, k_T)
            eng.wait_ge(unit_copied, 4 * KT)
            eng.wait_ge(codes_read, EB // 4)
            for g in range(4):
                rows = slice(DH * (g % 2), DH * (g % 2) + DH)
                for h in range(G4):
                    k = (g // 2) * G4 + h
                    last = eng.matmul(wide(SCORE_BANK[g], N)[:, h, :], q2_T[rows, k, :], k2_T[rows, k, :],
                                      start=True, stop=True)
                last.then_inc(scores_ready, 1)
            project(4, norm_T)
            turn_attn(0)
            turn_attn(1)
            eng.wait_ge(unit_copied, 5 * KT)
            project_rows(5, v_T, 2)
            turn_attn(2)
            turn_attn(3)
            eng.wait_ge(v2_ready, 2)
            for half in range(2):
                eng.wait_ge(attn_T_ready, 2 * half + 2)
                for k in range(G4):
                    for odd in range(2):
                        h = 2 * (half * G4 + k) + odd
                        last = eng.matmul(wide(4 + half)[DH * odd:DH * odd + DH, k, :], v2_rows[:, h * DH:h * DH + DH],
                                          attn_T[:, 2 * half + odd, k, :], start=True, stop=True)
                last.then_inc(heads_done, 1)
            eng.wait_ge(heads_ready, 2)
            project_rows(6, heads_T, 0)
            turn_rows(1)
            eng.wait_ge(norm_T_ready, 4)
            eng.wait_ge(router_landed, 16)
            for k in range(KT):
                last = eng.matmul(bank[6][0:N, 0:NE], norm_T[:, k, :], router_w[:, k, :],
                                  start=(k == 0), stop=(k == KT - 1))
            last.then_inc(logits_ready, 1)
            for b in (4, 5):
                eng.matmul(bank[b][:, 0:G4 * N], zeros[:, 0:P], zeros[:, :], start=True, stop=True)

            def spread_gate(e):
                eng.matmul(bank[7][:, 0:N], ones[:, :], gate_diag[:, e, :],
                           start=True, stop=True).then_inc(gate_spread, 1)

            def gate_up(u):
                w = ring[:, slot_of(u), 0:2 * UNIT].rearrange("p (a k o) -> p a k o", a=2, k=KT)
                for a in range(2):
                    for k in range(KT):
                        last = eng.matmul(bank[2 * (u % 2) + a][:, 0:N], w[:, a, k, :], norm_T[:, k, :],
                                          start=(k == 0), stop=(k == KT - 1))
                last.then_inc(tile_ready, 1)

            def down(u):
                w = ring[:, slot_of(u), 2 * UNIT:3 * UNIT].rearrange("p (m o) -> p m o", m=KT)
                for m in range(KT):
                    last = eng.matmul(wide(4 + m // G4)[:, m % G4, :], w[:, m, :], inner_T[:, u % 3, :],
                                      start=False, stop=False, skip_group_check=True)
                last.then_inc(down_done, 1)

            eng.wait_ge(landed[slot_of(0)], 16 * round_of(0))
            gate_up(0)
            eng.wait_ge(diag_ready, 1)
            spread_gate(0)

            def turn(i, last_turn):
                for u in range(U):
                    if not (last_turn and u == U - 1):
                        eng.wait_ge(landed[slot_of(u + 1)], i * 16 + 16 * round_of(u + 1))
                        eng.wait_ge(inner_ready, i * U + u)
                        gate_up((u + 1) % U)
                    if u % TILES == 2:
                        e = u // TILES
                        eng.wait_ge(diag_ready, i * 2 + (e + 2))
                        eng.wait_ge(gate_ready, i * 2 + (e + 1))
                        spread_gate((e + 1) % 2)
                    eng.wait_ge(inner_ready, i * U + (u + 1))
                    down(u)

            with eng.Fori(0, TURNS - 1) as i:
                turn(i, False)
            turn(TURNS - 1, True)

            for half in range(2):
                eng.wait_ge(y_ready, half + 1)
                for m in range(G4):
                    last = eng.transpose(bank[half][0:N, m * P:m * P + P], y_T[:, half * G4 + m, :], ident[:, :])
                last.then_inc(y_turned, 1)


def kernel(x, src, dst, edge_type_5, L0_gnn_edge_type_weights, L0_gnn_wq, L0_gnn_bq, L0_gnn_wk, L0_gnn_bk,
           L0_gnn_wv, L0_gnn_bv, L0_gnn_wiq, L0_gnn_biq, L0_gnn_wik, L0_gnn_bik, L0_gnn_wiv, L0_gnn_biv,
           L0_gnn_wo, L0_gnn_bo, L0_ffn_gate, L0_ffn_gate_up_proj, L0_ffn_down_proj):
    import concourse.bacc as bacc
    from concourse.bass_utils import run_bass_kernel_spmd as run

    def tiles(w):
        return w.reshape(w.shape[0] // P, P, w.shape[1] // P, P).transpose(0, 3, 2, 1)

    def columns(v):
        return v.reshape(-1, P).T

    def edge_columns(v):
        return v.reshape(EB, P).T

    mats = [L0_gnn_wq, L0_gnn_wk, L0_gnn_wiq, L0_gnn_wik, L0_gnn_wv, L0_gnn_wiv, L0_gnn_wo]
    gnn_stream = np.concatenate([tiles(np.asarray(w)).reshape(KT, P, UNIT) for w in mats], axis=0)
    gu = np.asarray(L0_ffn_gate_up_proj).reshape(NE, 2, TILES, P, KT, P).transpose(0, 2, 5, 1, 4, 3)
    dn = np.asarray(L0_ffn_down_proj).reshape(NE, KT, P, TILES, P).transpose(0, 3, 4, 1, 2)
    expert_stream = np.concatenate([gu.reshape(T, P, 2 * UNIT), dn.reshape(T, P, UNIT)], axis=2)
    arrays = {
        "x": np.asarray(x),
        "edges": np.stack([edge_columns(np.asarray(v)) for v in (src, dst, edge_type_5)], axis=1),
        "edge_type_weights": np.asarray(L0_gnn_edge_type_weights),
        "bias_cols": np.stack([columns(np.asarray(v)) for v in (L0_gnn_bq, L0_gnn_bk, L0_gnn_biq, L0_gnn_bik,
                                                                L0_gnn_bv)], axis=1),
        "biv": np.asarray(L0_gnn_biv),
        "bo": np.asarray(L0_gnn_bo),
        "gnn_stream": gnn_stream,
        "gate_w": np.asarray(L0_ffn_gate).reshape(NE, KT, P).transpose(2, 1, 0),
        "expert_stream": expert_stream,
    }
    nc = bacc.Bacc("TRN2", target_bir_lowering=False, num_devices=1)
    feeds, args = {}, []
    for name, a in arrays.items():
        a = np.ascontiguousarray(a)
        feeds[f"in_{name}"] = a
        args.append(nc.dram_tensor(f"in_{name}", a.shape, mybir.dt.from_np(a.dtype), kind="ExternalInput").ap())
    args.append(nc.dram_tensor("out_0", (N, D), F32, kind="ExternalOutput").ap())
    gnn_moe_kernel(nc, *args)
    r = run(nc, [feeds], core_ids=[0])
    return r.results[0]["out_0"]
```

```python
import numpy as np

import concourse.bass as bass
from concourse import mybir
from contextlib import ExitStack

F32 = mybir.dt.float32
F32R = mybir.dt.float32r
BF16 = mybir.dt.bfloat16
I32 = mybir.dt.int32
ALU = mybir.AluOpType
ACT = mybir.ActivationFunctionType
AX = mybir.AxisListType

P = 128
N = 96
D = 1024
KT = D // P
DH = 64
EDGES = 3072
EB = EDGES // P
NE, INTER = 64, 768
WIDE = 512
UNIT = KT * P
PIECE = 2 * UNIT
SLOTS = 12
SPLITS = 3
GNN_UNITS = 7 * KT
GNN_PIECES = GNN_UNITS // 2
GROUP = 256
KG = GROUP // P
PER = INTER // GROUP
Q = NE * PER
PIECES = 3 * Q
STEPS = 12
TURNS = Q // STEPS
G4 = 4
EPS = 1e-5
ABSENT = -3.0e38
assert 3 * STEPS % SLOTS == 0 and STEPS % PER == 0 and STEPS % 2 == 0 and Q % STEPS == 0


def gnn_moe_kernel(nc, x, edges, edge_type_weights, bias_cols, biv, bo, gnn_stream, gate_w, expert_stream, out):
    ctx = ExitStack()
    with ctx:
        def sb(name, shape, dt=F32):
            return ctx.enter_context(nc.sbuf_tensor(name, shape, dt))

        def sem(name):
            return ctx.enter_context(nc.semaphore(name))

        ring = sb("ring", [P, SLOTS, PIECE])
        high = sb("high", [P, SPLITS, PIECE], F32R)
        low = sb("low", [P, SPLITS, PIECE], F32R)
        x_rows = sb("x_rows", [N, D])
        x1_rows = sb("x1_rows", [N, D])
        norm_rows = sb("norm_rows", [N, D])
        norm_T = sb("norm_T", [P, KT, N])
        q_T = sb("q_T", [P, KT, N])
        k_T = sb("k_T", [P, KT, N])
        q2_T = sb("q2_T", [P, KT, N])
        k2_T = sb("k2_T", [P, KT, N])
        v2_rows = norm_rows
        norm2_rows = x_rows
        v_T = k_T
        heads_T = q_T
        out_rows = v2_rows
        attn = sb("attn", [N, 4, G4, N])
        arena = sb("arena", [P, EB * N])
        pair_hit = arena[:, 0:EB * P // 2].bitcast(BF16).rearrange("p (b f) -> p b f", b=EB)
        src_hot = arena[:, 0:EB * N // 2].bitcast(BF16).rearrange("p (b n) -> p b n", b=EB)
        dst_hot = arena[:, EB * N // 2:EB * N].bitcast(BF16).rearrange("p (b n) -> p b n", b=EB)
        attn_T = arena[0:N, 0:4 * G4 * N].rearrange("p (g h n) -> p g h n", g=4, h=G4)
        router_w = sb("router_w", [P, KT, NE])
        bias_sb = sb("bias_sb", [P, 5, KT])
        ident = sb("ident", [P, P])
        later = sb("later", [P, P])
        zeros = sb("zeros", [P, WIDE], BF16)
        table_touch = sb("table_touch", [P, 3])
        node_id = sb("node_id", [P, N])
        block8 = sb("block8", [P, EB])
        edges_i = sb("edges_i", [P, 3, EB], I32)
        edges_f = sb("edges_f", [P, 3, EB])
        pair_key = sb("pair_key", [P, EB])
        edge_code = sb("edge_code", [P, EB])
        shadowed = sb("shadowed", [P, EB])
        code_part = sb("code_part", [N, 6, N])
        code_f = sb("code_f", [N, N])
        code_i = sb("code_i", [N, N], I32)
        mask = sb("mask", [N, N])
        etw = sb("etw", [N, 4])
        etw_abs = sb("etw_abs", [N, 4])
        etw_relu = sb("etw_relu", [N, 4])
        stats = sb("stats", [N, 2, 6])
        mean_var = sb("mean_var", [N, 2])
        ln_tmp = sb("ln_tmp", [N, 4])
        head_max = sb("head_max", [N, 4, G4])
        head_sum = sb("head_sum", [N, 4, G4])
        route = sb("route", [N, 3, NE])
        route_s = sb("route_s", [N, 6])
        top8 = sb("top8", [N, 8])
        route_w = sb("route_w", [N, NE])
        z_high = sb("z_high", [P, KT, N], F32R)
        z_low = sb("z_low", [P, KT, N], F32R)
        silu_rows = sb("silu_rows", [N, GROUP])
        inner_rows = sb("inner_rows", [N, GROUP])
        inner_high = sb("inner_high", [P, 2, KG, N], F32R)
        inner_low = sb("inner_low", [P, 2, KG, N], F32R)

        bank = [ctx.enter_context(nc.psum_tensor(f"bank{i}", [P, WIDE], F32)) for i in range(8)]

        def wide(b, rows=P):
            return bank[b][0:rows, 0:G4 * N].rearrange("p (g n) -> p g n", g=G4)

        def turned(u):
            return bank[2 + u % 2][:, 0:KG * N].rearrange("p (k n) -> p k n", k=KG)

        SCORE_BANK = [4, 6, 5, 7]

        landed = [sem(f"landed{s}") for s in range(SLOTS)]
        tail_landed = sem("tail_landed")
        x_landed = sem("x_landed")
        edges_landed = sem("edges_landed")
        etw_landed = sem("etw_landed")
        bias_landed = sem("bias_landed")
        bo_landed = sem("bo_landed")
        biv_landed = sem("biv_landed")
        router_landed = sem("router_landed")
        const_ready = sem("const_ready")
        pool_step = sem("pool_step")
        vector_step = sem("vector_step")
        scalar_step = sem("scalar_step")
        key_ready = sem("key_ready")
        pairs_ready = sem("pairs_ready")
        pairs_read = sem("pairs_read")
        onehot_ready = sem("onehot_ready")
        codes_ready = sem("codes_ready")
        codes_read = sem("codes_read")
        etw_abs_ready = sem("etw_abs_ready")
        softplus_ready = sem("softplus_ready")
        var_ready = sem("var_ready")
        std_ready = sem("std_ready")
        norm_ready = sem("norm_ready")
        norm_turned = sem("norm_turned")
        norm_T_ready = sem("norm_T_ready")
        unit_done = sem("unit_done")
        unit_copied = sem("unit_copied")
        scores_ready = sem("scores_ready")
        shifted = sem("shifted")
        exps_ready = sem("exps_ready")
        attn_ready = sem("attn_ready")
        attn_turned = sem("attn_turned")
        attn_T_ready = sem("attn_T_ready")
        v2_ready = sem("v2_ready")
        heads_done = sem("heads_done")
        heads_ready = sem("heads_ready")
        logits_ready = sem("logits_ready")
        logits_shift = sem("logits_shift")
        logits_exp = sem("logits_exp")
        z_high_ready = sem("z_high_ready")
        z_low_ready = sem("z_low_ready")
        high_ready = sem("high_ready")
        low_ready = sem("low_ready")
        piece_done = sem("piece_done")
        silu_ready = sem("silu_ready")
        inner_ready = sem("inner_ready")
        inner_turned = sem("inner_turned")
        inner_high_ready = sem("inner_high_ready")
        inner_low_ready = sem("inner_low_ready")
        out_ready = sem("out_ready")
        stored = sem("stored")

        block = ctx.enter_context(nc.Block())

        def slot_of(p):
            return (GNN_PIECES + p) % SLOTS

        def loads_of(p):
            return (GNN_PIECES + p) // SLOTS + 1

        LAST = PIECES - 1
        HALF = [slice(0, PIECE // 2), slice(PIECE // 2, PIECE)]
        last_landed = [(landed[slot_of(LAST)], 16 * loads_of(LAST)), (tail_landed, 16)]
        TURN_LOADS = 3 * STEPS // SLOTS

        def gate_up_pieces(u):
            return 3 * u + 2, 3 * u + 3

        def down_piece(u):
            return 3 * u + 4

        @block.sync
        def _(eng):
            eng.dma_start(x_rows[:, :], x).then_inc(x_landed, 16)
            for c in range(GNN_PIECES):
                if c >= SLOTS:
                    eng.wait_ge(unit_done, 2 * (c - SLOTS + 1))
                eng.dma_start(ring[:, c % SLOTS, :].rearrange("p (u f) -> p u f", u=2),
                              gnn_stream[2 * c:2 * c + 2].rearrange("u p f -> p u f")).then_inc(landed[c % SLOTS], 16)

            for p in range(SLOTS):
                eng.wait_ge(unit_done, 2 * (GNN_PIECES + p - SLOTS + 1))
                eng.dma_start(ring[:, slot_of(p), :], expert_stream[p]).then_inc(landed[slot_of(p)], 16)
            with eng.Fori(1, PIECES // SLOTS - 1) as i:
                for p in range(SLOTS):
                    eng.wait_ge(low_ready, i * SLOTS + (p - SLOTS + 1))
                    eng.dma_start(ring[:, slot_of(p), :],
                                  expert_stream[bass.ds(i * SLOTS + p, 1)].rearrange("u p f -> p (u f)"))\
                       .then_inc(landed[slot_of(p)], 16)
            for p in range(PIECES - SLOTS, LAST):
                eng.wait_ge(low_ready, p - SLOTS + 1)
                eng.dma_start(ring[:, slot_of(p), :], expert_stream[p]).then_inc(landed[slot_of(p)], 16)
            eng.wait_ge(low_ready, LAST - SLOTS + 1)
            eng.dma_start(ring[:, slot_of(LAST), HALF[0]], expert_stream[LAST][:, HALF[0]])\
               .then_inc(landed[slot_of(LAST)], 16)
            eng.dma_start(ring[:, slot_of(LAST), HALF[1]], expert_stream[LAST][:, HALF[1]]).then_inc(tail_landed, 16)
            for half in range(2):
                eng.wait_ge(out_ready, half + 1)
                cols = slice(half * WIDE, half * WIDE + WIDE)
                eng.dma_start(out[:, cols], out_rows[:, cols]).then_inc(stored, 16)
            eng.wait_ge(stored, 32)

        @block.gpsimd
        def _(eng):
            eng.memset(ident[:, :], 0.0).then_inc(pool_step, 1)
            eng.memset(later[:, :], 1.0).then_inc(pool_step, 1)
            eng.memset(zeros[:, :], 0.0).then_inc(const_ready, 1)
            eng.iota(node_id[:, :], pattern=[[1, N]], base=0, channel_multiplier=0,
                     allow_small_or_imprecise_dtypes=True).then_inc(const_ready, 1)
            eng.iota(block8[:, :], pattern=[[8, EB]], base=8, channel_multiplier=0,
                     allow_small_or_imprecise_dtypes=True).then_inc(const_ready, 1)
            eng.wait_ge(pool_step, 2)
            eng.affine_select(out=ident[:, :], in_=ident[:, :], compare_op=ALU.not_equal, fill=1.0, base=0,
                              pattern=[[-1, P]], channel_multiplier=1).then_inc(const_ready, 1)
            eng.affine_select(out=later[:, :], in_=later[:, :], compare_op=ALU.is_gt, fill=0.0, base=0,
                              pattern=[[1, P]], channel_multiplier=-1).then_inc(const_ready, 1)

        CONSTS = 5

        @block.scalar
        def _(eng):
            eng.dma_start(edges_i[:, :, :], edges).then_inc(edges_landed, 16)
            eng.dma_start(etw[:, :], edge_type_weights.partition_broadcast(N)).then_inc(etw_landed, 16)
            eng.dma_start(bias_sb[:, :, :], bias_cols).then_inc(bias_landed, 16)
            eng.dma_start(x1_rows[:, :], bo.partition_broadcast(N)).then_inc(bo_landed, 16)
            eng.dma_start(router_w[:, :, :], gate_w).then_inc(router_landed, 16)
            eng.wait_ge(const_ready, CONSTS)

            def split_high(i, p):
                eng.wait_ge(landed[slot_of(p)], i * (16 * TURN_LOADS) + 16 * loads_of(p))
                if not (isinstance(i, int) and i * 3 * STEPS + p < SPLITS):
                    eng.wait_ge(piece_done, i * (3 * STEPS) + (p - SPLITS + 1))
                eng.copy(high[:, p % SPLITS, :], ring[:, slot_of(p), :]).then_inc(high_ready, 1)

            def load_table(n, func):
                eng.activation(table_touch[:, n:n + 1], zeros[:, 0:1], func)

            def std(n):
                eng.wait_ge(var_ready, n)
                eng.activation(ln_tmp[:, 1:2], ln_tmp[:, 0:1], ACT.Sqrt).then_inc(std_ready, 1)

            def copy_norm_T():
                for half in range(2):
                    part = slice(half * G4, half * G4 + G4)
                    eng.copy(norm_T[:, part, :], wide(2 + half)).then_inc(norm_T_ready, 1)

            std(1)
            eng.wait_ge(norm_turned, 1)
            eng.copy(norm_T[:, 0:G4, :], wide(2)).then_inc(norm_T_ready, 1)
            eng.wait_ge(norm_turned, 2)
            eng.dma_start(v2_rows[:, :], biv.partition_broadcast(N)).then_inc(biv_landed, 16)

            eng.wait_ge(bias_landed, 16)
            matrices = [(q_T, 0), (k_T, 1), (q2_T, 2), (k2_T, 3), (v_T, 4)]

            def copy_units(g):
                dest, b = matrices[g]
                for m in range(KT):
                    u = g * KT + m
                    eng.wait_ge(unit_done, u + 1)
                    eng.activation(dest[:, m, :], bank[u % 4][:, 0:N], ACT.Identity,
                                   bias=bias_sb[:, b, m:m + 1]).then_inc(unit_copied, 1)

            copy_units(0)
            eng.wait_ge(etw_abs_ready, 1)
            eng.activation(etw_abs[:, :], etw_abs[:, :], ACT.Exp, scale=-1.0).then_inc(scalar_step, 1)
            eng.wait_ge(scalar_step, 1)
            eng.activation(etw_abs[:, :], etw_abs[:, :], ACT.Ln, bias=1.0).then_inc(softplus_ready, 1)
            for g in range(1, 4):
                copy_units(g)
            dest, b = matrices[4]
            for m in range(KT):
                if m % 2 == 1:
                    g = m // 2
                    eng.wait_ge(shifted, g + 1)
                    eng.activation(attn[:, g, :, :], attn[:, g, :, :], ACT.Exp).then_inc(exps_ready, 1)
                u = 4 * KT + m
                eng.wait_ge(unit_done, u + 1)
                eng.activation(dest[:, m, :], bank[u % 4][:, 0:N], ACT.Identity,
                               bias=bias_sb[:, b, m:m + 1]).then_inc(unit_copied, 1)
            for g in range(4):
                if g == 2:
                    for p in range(SPLITS):
                        split_high(0, p)
                eng.wait_ge(attn_turned, g + 1)
                eng.copy(attn_T[:, g, :, :], wide(SCORE_BANK[g], N)).then_inc(attn_T_ready, 1)
            load_table(0, ACT.Sqrt)
            for half in range(2):
                eng.wait_ge(heads_done, half + 1)
                eng.copy(heads_T[:, half * G4:half * G4 + G4, :], wide(4 + half)).then_inc(heads_ready, 1)

            std(2)
            for half in range(2):
                eng.wait_ge(norm_turned, 3 + half)
                eng.copy(z_high[:, half * G4:half * G4 + G4, :], wide(2 + half)).then_inc(z_high_ready, 1)
            eng.wait_ge(z_low_ready, 2)
            copy_norm_T()
            load_table(1, ACT.Exp)
            split_high(0, SPLITS)
            eng.wait_ge(logits_shift, 1)
            eng.activation(route[:, 1, :], route[:, 0, :], ACT.Exp, accum_out=route_s[:, 1:2]).then_inc(logits_exp, 1)
            load_table(2, ACT.Silu)

            def turn(i, first, last):
                for u in range(STEPS):
                    ends = last and u == STEPS - 1
                    if not ends and not (first and u == 0):
                        split_high(i, gate_up_pieces(u)[0])
                    if ends:
                        eng.wait_ge(piece_done, LAST - SPLITS + 1)
                        for half in range(2):
                            eng.wait_ge(*last_landed[half])
                            eng.copy(high[:, LAST % SPLITS, HALF[half]], ring[:, slot_of(LAST), HALF[half]])\
                               .then_inc(high_ready, 1)
                    eng.wait_ge(piece_done, 2 if first and u == 0 else i * (3 * STEPS) + (3 * u + 1))
                    if not (first and u == 0):
                        eng.wait_ge(inner_ready, i * STEPS + u)
                    eng.activation(silu_rows[:, :], bank[u % 2][0:N, 0:GROUP], ACT.Silu).then_inc(silu_ready, 1)
                    if not ends and not (first and u == 0):
                        split_high(i, gate_up_pieces(u)[1])
                    if not ends:
                        split_high(i, down_piece(u))
                    eng.wait_ge(inner_turned, i * STEPS + (u + 1))
                    eng.copy(inner_high[:, u % 2, :, :], turned(u)).then_inc(inner_high_ready, 1)

            turn(0, True, False)
            with eng.Fori(1, TURNS - 1) as i:
                turn(i, False, False)
            turn(TURNS - 1, False, True)

        @block.vector
        def _(eng):
            steps = [0]

            def link(ins):
                steps[0] += 1
                ins.then_inc(vector_step, 1)
                eng.wait_ge(vector_step, steps[0])

            def split_low(i, p):
                eng.wait_ge(high_ready, i * (3 * STEPS) + (p + 1))
                eng.tensor_tensor(low[:, p % SPLITS, :], ring[:, slot_of(p), :], high[:, p % SPLITS, :].bitcast(F32),
                                  ALU.subtract).then_inc(low_ready, 1)

            def row_stats(rows, half):
                link(eng.bn_stats(stats[:, half, :], rows[:, half * WIDE:half * WIDE + WIDE]))

            def layernorm(n, rows, result):
                link(eng.bn_aggr(mean_var[:, :], stats[:, :, :].rearrange("p a b -> p (a b)")))
                eng.tensor_scalar(ln_tmp[:, 0:1], mean_var[:, 1:2], EPS, None, ALU.add).then_inc(var_ready, 1)
                eng.wait_ge(std_ready, n)
                link(eng.reciprocal(ln_tmp[:, 2:3], ln_tmp[:, 1:2]))
                link(eng.tensor_scalar(ln_tmp[:, 3:4], ln_tmp[:, 2:3], ln_tmp[:, 2:3], ln_tmp[:, 0:1],
                                       ALU.mult, ALU.mult))
                link(eng.tensor_scalar(ln_tmp[:, 3:4], ln_tmp[:, 3:4], -0.5, 1.5, ALU.mult, ALU.add))
                link(eng.tensor_tensor(ln_tmp[:, 2:3], ln_tmp[:, 2:3], ln_tmp[:, 3:4], ALU.mult))
                for half in range(2):
                    cols = slice(half * WIDE, half * WIDE + WIDE)
                    eng.tensor_scalar(result[:, cols], rows[:, cols], mean_var[:, 0:1], ln_tmp[:, 2:3],
                                      ALU.subtract, ALU.mult).then_inc(norm_ready, 1)

            eng.wait_ge(edges_landed, 16)
            link(eng.tensor_copy(edges_f[:, :, :], edges_i[:, :, :]))
            src, dst, kind = edges_f[:, 0, :], edges_f[:, 1, :], edges_f[:, 2, :]
            eng.scalar_tensor_tensor(pair_key[:, :], src, float(N), dst, ALU.mult, ALU.add).then_inc(key_ready, 1)
            eng.wait_ge(x_landed, 16)
            for half in range(2):
                row_stats(x_rows, half)
            layernorm(1, x_rows, norm_rows)
            eng.wait_ge(norm_turned, 2)
            eng.tensor_copy(norm_T[:, G4:2 * G4, :], wide(3)).then_inc(norm_T_ready, 1)
            eng.wait_ge(etw_landed, 16)
            link(eng.tensor_scalar(etw_relu[:, :], etw[:, :], 0.0, None, ALU.max))
            eng.scalar_tensor_tensor(etw_abs[:, :], etw_relu[:, :], 2.0, etw[:, :], ALU.mult,
                                     ALU.subtract).then_inc(etw_abs_ready, 1)

            eng.wait_ge(const_ready, CONSTS)
            eng.wait_ge(key_ready, 1)
            for g in range(EB // 4):
                eng.wait_ge(pairs_ready, g + 1)
                for k in range(4):
                    b = 4 * g + k
                    last = eng.scalar_tensor_tensor(pair_hit[:, b, :], bank[4 + g % 4][:, k * P:k * P + P],
                                                    pair_key[:, b:b + 1], later[:, :], ALU.is_equal, ALU.mult,
                                                    accum_out=shadowed[:, b:b + 1])
                last.then_inc(pairs_read, 1)
            link(eng.tensor_scalar(edge_code[:, :], kind, 0.0, 4.0, ALU.is_equal, ALU.mult))
            link(eng.tensor_tensor(edge_code[:, :], edge_code[:, :], kind, ALU.add))
            link(eng.tensor_tensor(edge_code[:, :], edge_code[:, :], block8[:, :], ALU.add))
            eng.wait_ge(pairs_read, EB // 4)
            link(eng.scalar_tensor_tensor(edge_code[:, :], shadowed[:, :], 0.0, edge_code[:, :],
                                          ALU.is_equal, ALU.mult))
            node = node_id[:, :].unsqueeze(1).to_broadcast([P, EB, N])
            eng.tensor_tensor(src_hot, node, src.unsqueeze(2).to_broadcast([P, EB, N]),
                              ALU.is_equal).then_inc(onehot_ready, 1)
            link(eng.tensor_tensor(dst_hot, node, dst.unsqueeze(2).to_broadcast([P, EB, N]), ALU.is_equal))
            eng.tensor_tensor(dst_hot, dst_hot, edge_code[:, :].unsqueeze(2).to_broadcast([P, EB, N]),
                              ALU.mult).then_inc(onehot_ready, 1)
            eng.wait_ge(bo_landed, 16)
            link(eng.tensor_tensor(x1_rows[:, :], x1_rows[:, :], x_rows[:, :], ALU.add))
            for g in range(EB // 4):
                eng.wait_ge(codes_ready, g + 1)
                eng.tensor_reduce(code_part[:, g, :], wide(4 + g % 4, N).rearrange("p g n -> p n g"), AX.X,
                                  ALU.max).then_inc(codes_read, 1)
            eng.wait_ge(codes_read, EB // 4)
            link(eng.tensor_reduce(code_f[:, :], code_part[:, :, :].rearrange("p g n -> p n g"), AX.X, ALU.max))
            link(eng.scalar_tensor_tensor(code_f[:, :], ident[0:N, 0:N], 4.0, code_f[:, :], ALU.mult, ALU.max))
            link(eng.tensor_copy(code_i[:, :], code_f[:, :]))
            link(eng.tensor_scalar(code_i[:, :], code_i[:, :], 7, None, ALU.bitwise_and))
            link(eng.tensor_copy(code_f[:, :], code_i[:, :]))
            eng.wait_ge(softplus_ready, 1)
            link(eng.tensor_tensor(etw[:, :], etw_abs[:, :], etw_relu[:, :], ALU.add))
            link(eng.tensor_scalar(mask[:, :], code_f[:, :], 0.0, ABSENT, ALU.is_equal, ALU.mult))
            for c in range(1, 5):
                pick = attn[:, 0, c - 1, :]
                link(eng.tensor_scalar(pick, code_f[:, :], float(c), etw[:, c - 1:c], ALU.is_equal, ALU.mult))
                link(eng.tensor_tensor(mask[:, :], mask[:, :], pick, ALU.add))

            for g in range(4):
                eng.wait_ge(scores_ready, g + 1)
                link(eng.scalar_tensor_tensor(attn[:, g, :, :], wide(SCORE_BANK[g], N), float(DH) ** -0.5,
                                              mask[:, :].unsqueeze(1).to_broadcast([N, G4, N]),
                                              ALU.mult, ALU.add))
                link(eng.tensor_reduce(head_max[:, g, :], attn[:, g, :, :], AX.X, ALU.max))
                eng.tensor_tensor(attn[:, g, :, :], attn[:, g, :, :],
                                  head_max[:, g, :].unsqueeze(2).to_broadcast([N, G4, N]),
                                  ALU.subtract).then_inc(shifted, 1)
            for g in range(4):
                eng.wait_ge(exps_ready, g + 1)
                link(eng.tensor_reduce(head_sum[:, g, :], attn[:, g, :, :], AX.X, ALU.add))
                link(eng.reciprocal(head_sum[:, g, :], head_sum[:, g, :]))
                eng.tensor_tensor(attn[:, g, :, :], attn[:, g, :, :],
                                  head_sum[:, g, :].unsqueeze(2).to_broadcast([N, G4, N]),
                                  ALU.mult).then_inc(attn_ready, 1)

            for p in range(SPLITS):
                split_low(0, p)
            eng.wait_ge(biv_landed, 16)
            for half in range(2):
                cols = slice(half * WIDE, half * WIDE + WIDE)
                eng.wait_ge(unit_done, 5 * KT + 4 * (half + 1))
                eng.tensor_tensor(v2_rows[:, cols], bank[2 + half][0:N, :], v2_rows[:, cols],
                                  ALU.add).then_inc(v2_ready, 1)
            for half in range(2):
                cols = slice(half * WIDE, half * WIDE + WIDE)
                eng.wait_ge(unit_done, 6 * KT + 4 * (half + 1))
                link(eng.tensor_tensor(x1_rows[:, cols], bank[half][0:N, :], x1_rows[:, cols], ALU.add))
                row_stats(x1_rows, half)
            layernorm(2, x1_rows, norm2_rows)
            for half in range(2):
                part = slice(half * G4, half * G4 + G4)
                eng.wait_ge(z_high_ready, half + 1)
                eng.tensor_tensor(z_low[:, part, :], wide(2 + half), z_high[:, part, :].bitcast(F32),
                                  ALU.subtract).then_inc(z_low_ready, 1)

            split_low(0, SPLITS)
            eng.wait_ge(logits_ready, 1)
            link(eng.tensor_reduce(route_s[:, 0:1], bank[6][0:N, 0:NE], AX.X, ALU.max))
            eng.tensor_scalar(route[:, 0, :], bank[6][0:N, 0:NE], route_s[:, 0:1], None,
                              ALU.subtract).then_inc(logits_shift, 1)
            eng.wait_ge(logits_exp, 1)
            link(eng.reciprocal(route_s[:, 2:3], route_s[:, 1:2]))
            link(eng.tensor_scalar(route[:, 0, :], route[:, 1, :], route_s[:, 2:3], None, ALU.mult))
            link(eng.max(top8[:, :], route[:, 0, :]))
            link(eng.match_replace(route[:, 2, :], top8[:, :], route[:, 0, :], -1.0))
            link(eng.tensor_reduce(route_s[:, 3:4], top8[:, :], AX.X, ALU.add))
            link(eng.reciprocal(route_s[:, 4:5], route_s[:, 3:4]))
            link(eng.scalar_tensor_tensor(route[:, 1, :], route[:, 2, :], 0.0, route[:, 0, :], ALU.is_lt, ALU.mult))
            link(eng.tensor_scalar(route_w[:, :], route[:, 1, :], route_s[:, 4:5], None, ALU.mult))

            def turn(i, first, last):
                for u in range(STEPS):
                    ends = last and u == STEPS - 1
                    if not ends and not (first and u == 0):
                        split_low(i, gate_up_pieces(u)[0])
                    if ends:
                        for half in range(2):
                            eng.wait_ge(high_ready, LAST + 1 + half)
                            eng.tensor_tensor(low[:, LAST % SPLITS, HALF[half]], ring[:, slot_of(LAST), HALF[half]],
                                              high[:, LAST % SPLITS, HALF[half]].bitcast(F32),
                                              ALU.subtract).then_inc(low_ready, 1)
                    eng.wait_ge(silu_ready, i * STEPS + (u + 1))
                    if not (first and u == 0):
                        eng.wait_ge(inner_turned, i * STEPS + u)
                    e = u // PER
                    w = route_w[:, e:e + 1] if first else route_w[:, bass.ds(i * (STEPS // PER) + e, 1)]
                    eng.scalar_tensor_tensor(inner_rows[:, :], bank[u % 2][0:N, GROUP:2 * GROUP], w, silu_rows[:, :],
                                             ALU.mult, ALU.mult).then_inc(inner_ready, 1)
                    if not ends and not (first and u == 0):
                        split_low(i, gate_up_pieces(u)[1])
                    if not ends:
                        split_low(i, down_piece(u))
                    eng.wait_ge(inner_high_ready, i * STEPS + (u + 1))
                    eng.tensor_tensor(inner_low[:, u % 2, :, :], turned(u), inner_high[:, u % 2, :, :].bitcast(F32),
                                      ALU.subtract).then_inc(inner_low_ready, 1)
            turn(0, True, False)
            with eng.Fori(1, TURNS - 1) as i:
                turn(i, False, False)
            turn(TURNS - 1, False, True)

            for half in range(2):
                eng.wait_ge(piece_done, PIECES + half)
                cols = slice(half * WIDE, half * WIDE + WIDE)
                eng.tensor_tensor(out_rows[:, cols], bank[4 + half][0:N, :], x1_rows[:, cols],
                                  ALU.add).then_inc(out_ready, 1)

        @block.tensor
        def _(eng):
            def turn_rows(n, rows):
                for half in range(2):
                    eng.wait_ge(norm_ready, 2 * n + half + 1)
                    for m in range(G4):
                        k = half * G4 + m
                        last = eng.transpose(wide(2 + half)[:, m, :], rows[:, k * P:k * P + P], ident[0:N, 0:N])
                    last.then_inc(norm_turned, 1)

            def spread_keys(g):
                if g >= 4:
                    eng.wait_ge(pairs_read, g - 3)
                for k in range(4):
                    b = 4 * g + k
                    last = eng.matmul(bank[4 + g % 4][:, k * P:k * P + P], pair_key[:, b:b + 1].to_broadcast([P, P]),
                                      ident[:, :], start=True, stop=True)
                last.then_inc(pairs_ready, 1)

            def place_codes(g):
                if g >= 4:
                    eng.wait_ge(codes_read, g - 3)
                for k in range(4):
                    b = 4 * g + k
                    last = eng.matmul(wide(4 + g % 4, N)[:, k, :], src_hot[:, b, :], dst_hot[:, b, :],
                                      start=True, stop=True)
                last.then_inc(codes_ready, 1)

            def unit_weights(u):
                c = u // 2
                eng.wait_ge(landed[c % SLOTS], 16 * (c // SLOTS + 1))
                return ring[:, c % SLOTS, (u % 2) * UNIT:(u % 2 + 1) * UNIT].rearrange("p (k o) -> p k o", k=KT)

            def project(g, src_T):
                for m in range(KT):
                    u = g * KT + m
                    if u >= 4:
                        eng.wait_ge(unit_copied, u - 3)
                    w = unit_weights(u)
                    for k in range(KT):
                        last = eng.matmul(bank[u % 4][:, 0:N], w[:, k, :], src_T[:, k, :],
                                          start=(k == 0), stop=(k == KT - 1))
                    last.then_inc(unit_done, 1)

            def project_rows(g, src_T, first_bank):
                for m in range(KT):
                    w = unit_weights(g * KT + m)
                    for k in range(KT):
                        last = eng.matmul(bank[first_bank + m // 4][0:N, (m % 4) * P:(m % 4 + 1) * P],
                                          src_T[:, k, :], w[:, k, :], start=(k == 0), stop=(k == KT - 1))
                    last.then_inc(unit_done, 1)

            def turn_attn(g):
                eng.wait_ge(attn_ready, g + 1)
                for h in range(G4):
                    last = eng.transpose(wide(SCORE_BANK[g], N)[:, h, :], attn[:, g, h, :], ident[0:N, 0:N])
                last.then_inc(attn_turned, 1)

            eng.wait_ge(const_ready, CONSTS)
            eng.wait_ge(key_ready, 1)
            for g in range(4):
                spread_keys(g)
            turn_rows(0, norm_rows)
            eng.wait_ge(norm_T_ready, 2)
            project(0, norm_T)
            project(1, norm_T)
            for g in range(4, EB // 4):
                spread_keys(g)
            eng.wait_ge(unit_copied, KT)
            project(2, q_T)
            eng.wait_ge(onehot_ready, 2)
            for g in range(4):
                place_codes(g)
            eng.wait_ge(unit_copied, 2 * KT)
            project(3, k_T)
            for g in range(4, EB // 4):
                place_codes(g)
            eng.wait_ge(unit_copied, 4 * KT)
            eng.wait_ge(codes_read, EB // 4)
            for g in range(4):
                rows = slice(DH * (g % 2), DH * (g % 2) + DH)
                for h in range(G4):
                    k = (g // 2) * G4 + h
                    last = eng.matmul(wide(SCORE_BANK[g], N)[:, h, :], q2_T[rows, k, :], k2_T[rows, k, :],
                                      start=True, stop=True)
                last.then_inc(scores_ready, 1)
            project(4, norm_T)
            turn_attn(0)
            turn_attn(1)
            eng.wait_ge(unit_copied, 5 * KT)
            project_rows(5, v_T, 2)
            turn_attn(2)
            turn_attn(3)
            eng.wait_ge(v2_ready, 2)
            for half in range(2):
                eng.wait_ge(attn_T_ready, 2 * half + 2)
                for k in range(G4):
                    for odd in range(2):
                        h = 2 * (half * G4 + k) + odd
                        last = eng.matmul(wide(4 + half)[DH * odd:DH * odd + DH, k, :], v2_rows[:, h * DH:h * DH + DH],
                                          attn_T[:, 2 * half + odd, k, :], start=True, stop=True)
                last.then_inc(heads_done, 1)
            eng.wait_ge(heads_ready, 2)
            project_rows(6, heads_T, 0)
            turn_rows(1, norm2_rows)
            for b in (4, 5):
                eng.matmul(bank[b][0:N, :], zeros[:, 0:N], zeros[:, :], start=True, stop=True)


            def gate_up(i, p, half, u):
                eng.wait_ge(low_ready, i * (3 * STEPS) + (p + 1))
                w_high = high[:, p % SPLITS, :].rearrange("p (k o) -> p k o", k=KT // 2)
                w_low = low[:, p % SPLITS, :].rearrange("p (k o) -> p k o", k=KT // 2)
                for k in range(KT // 2):
                    z = half * (KT // 2) + k
                    passes = [(z_high, w_high), (z_high, w_low), (z_low, w_high)]
                    for n, (a, w) in enumerate(passes):
                        last = eng.matmul(bank[u % 2][0:N, :], a[:, z, :], w[:, k, :],
                                          start=(half == 0 and k == 0 and n == 0),
                                          stop=(half == 1 and k == KT // 2 - 1 and n == 2))
                last.then_inc(piece_done, 1)

            def down(i, p, u):
                eng.wait_ge(low_ready, i * (3 * STEPS) + (p + 1))
                eng.wait_ge(inner_high_ready, i * STEPS + (u + 1))
                w_high = high[:, p % SPLITS, :].rearrange("p (k o) -> p k o", k=KG)
                w_low = low[:, p % SPLITS, :].rearrange("p (k o) -> p k o", k=KG)
                passes = [(inner_high, w_high), (inner_high, w_low), (inner_low, w_high)]
                for n, (a, w) in enumerate(passes):
                    if n == 2:
                        eng.wait_ge(inner_low_ready, i * STEPS + (u + 1))
                    for k in range(KG):
                        for half in range(2):
                            last = eng.matmul(bank[4 + half][0:N, :], a[:, u % 2, k, :],
                                              w[:, k, half * WIDE:half * WIDE + WIDE],
                                              start=False, stop=False, skip_group_check=True)
                last.then_inc(piece_done, 1)

            def last_down(u):
                eng.wait_ge(inner_low_ready, Q)
                for k in range(KG):
                    eng.wait_ge(low_ready, LAST + 1 + k)
                    w_high = high[:, LAST % SPLITS, HALF[k]]
                    w_low = low[:, LAST % SPLITS, HALF[k]]
                    for half in range(2):
                        cols = slice(half * WIDE, half * WIDE + WIDE)
                        for a, w in [(inner_high, w_high), (inner_high, w_low), (inner_low, w_high)]:
                            last = eng.matmul(bank[4 + half][0:N, :], a[:, u % 2, k, :], w[:, cols],
                                              start=False, stop=False, skip_group_check=True)
                        if k == KG - 1:
                            last.then_inc(piece_done, 1)

            def turn(i, first, last_turn):
                for u in range(STEPS):
                    ends = last_turn and u == STEPS - 1
                    if not ends:
                        if not (first and u == 0):
                            eng.wait_ge(inner_ready, i * STEPS + u)
                        gate_up(i, gate_up_pieces(u)[0], 0, u + 1)
                    eng.wait_ge(inner_ready, i * STEPS + (u + 1))
                    if not (first and u < 2):
                        eng.wait_ge(inner_low_ready, i * STEPS + (u - 1))
                    for k in range(KG):
                        last = eng.transpose(turned(u)[:, k, :], inner_rows[:, k * P:k * P + P], ident[0:N, 0:N])
                    last.then_inc(inner_turned, 1)
                    if not ends:
                        gate_up(i, gate_up_pieces(u)[1], 1, u + 1)
                    if not ends:
                        down(i, down_piece(u), u)

            eng.wait_ge(z_low_ready, 1)
            gate_up(0, 0, 0, 0)
            eng.wait_ge(norm_T_ready, 4)
            eng.wait_ge(router_landed, 16)
            for k in range(KT):
                last = eng.matmul(bank[6][0:N, 0:NE], norm_T[:, k, :], router_w[:, k, :],
                                  start=(k == 0), stop=(k == KT - 1))
            last.then_inc(logits_ready, 1)
            eng.wait_ge(z_low_ready, 2)
            gate_up(0, 1, 1, 0)
            turn(0, True, False)
            with eng.Fori(1, TURNS - 1) as i:
                turn(i, False, False)
            turn(TURNS - 1, False, True)
            last_down(STEPS - 1)


def kernel(x, src, dst, edge_type_5, L0_gnn_edge_type_weights, L0_gnn_wq, L0_gnn_bq, L0_gnn_wk, L0_gnn_bk,
           L0_gnn_wv, L0_gnn_bv, L0_gnn_wiq, L0_gnn_biq, L0_gnn_wik, L0_gnn_bik, L0_gnn_wiv, L0_gnn_biv,
           L0_gnn_wo, L0_gnn_bo, L0_ffn_gate, L0_ffn_gate_up_proj, L0_ffn_down_proj):
    import concourse.bacc as bacc
    from concourse.bass_utils import run_bass_kernel_spmd as run

    def tiles(w):
        return w.reshape(w.shape[0] // P, P, w.shape[1] // P, P).transpose(0, 3, 2, 1)

    def columns(v):
        return v.reshape(-1, P).T

    def edge_columns(v):
        return v.reshape(EB, P).T

    mats = [L0_gnn_wq, L0_gnn_wk, L0_gnn_wiq, L0_gnn_wik, L0_gnn_wv, L0_gnn_wiv, L0_gnn_wo]
    gnn_stream = np.concatenate([tiles(np.asarray(w)).reshape(KT, P, UNIT) for w in mats], axis=0)
    gu = np.asarray(L0_ffn_gate_up_proj).reshape(NE, 2, PER, GROUP, 2, KT // 2, P).transpose(0, 2, 4, 6, 5, 1, 3)
    gu = gu.reshape(Q, 2, P, PIECE)
    dn = np.asarray(L0_ffn_down_proj).reshape(NE, D, PER, KG, P).transpose(0, 2, 4, 3, 1).reshape(Q, 1, P, PIECE)
    steps = np.concatenate([gu[1:], dn[:-1]], axis=1).reshape(3 * (Q - 1), P, PIECE)
    expert_stream = np.concatenate([gu[0], steps, dn[-1]], axis=0)
    arrays = {
        "x": np.asarray(x),
        "edges": np.stack([edge_columns(np.asarray(v)) for v in (src, dst, edge_type_5)], axis=1),
        "edge_type_weights": np.asarray(L0_gnn_edge_type_weights),
        "bias_cols": np.stack([columns(np.asarray(v)) for v in (L0_gnn_bq, L0_gnn_bk, L0_gnn_biq, L0_gnn_bik,
                                                                L0_gnn_bv)], axis=1),
        "biv": np.asarray(L0_gnn_biv),
        "bo": np.asarray(L0_gnn_bo),
        "gnn_stream": gnn_stream,
        "gate_w": np.asarray(L0_ffn_gate).reshape(NE, KT, P).transpose(2, 1, 0),
        "expert_stream": expert_stream,
    }
    nc = bacc.Bacc("TRN2", target_bir_lowering=False, num_devices=1)
    feeds, args = {}, []
    for name, a in arrays.items():
        a = np.ascontiguousarray(a)
        feeds[f"in_{name}"] = a
        args.append(nc.dram_tensor(f"in_{name}", a.shape, mybir.dt.from_np(a.dtype), kind="ExternalInput").ap())
    args.append(nc.dram_tensor("out_0", (N, D), F32, kind="ExternalOutput").ap())
    gnn_moe_kernel(nc, *args)
    r = run(nc, [feeds], core_ids=[0])
    return r.results[0]["out_0"]
```
